# Optimizing a Trainium2 kernel written in Bass

```python
import numpy as np
import jax
import jax.numpy as jnp

def _softmax(x, axis=-1):
    return jax.nn.softmax(x, axis=axis)

def _gelu(x):
    return jax.nn.gelu(x, approximate=True)

def _silu(x):
    return jax.nn.silu(x)

def _sigmoid(x):
    return jax.nn.sigmoid(x)

def _layernorm(x, axis=-1, eps=1e-05):
    m = jnp.mean(x, axis=axis, keepdims=True)
    v = jnp.var(x, axis=axis, keepdims=True)
    return (x - m) / jnp.sqrt(v + eps)

def _scatter_add(tgt, idx, src, axis=0):
    return tgt.at[idx].add(src)

def _segment_sum(src, seg, n):
    return jax.ops.segment_sum(src, seg, n)
kernel_name = 'mk_cond_resid_d2_seqx_r4_1578d0'

def setup_inputs(seed: int=0):
    np.random.seed(seed)
    _w = jnp.asarray

    def _rec_inputs():
        import jax
        import jax.numpy as jnp
        _rk = jax.random.key(seed)
        x = 7.22e-05 + 1 * jax.random.normal(jax.random.fold_in(_rk, 1), (8, 256, 1024), jnp.float32)
        _lenS = 256 - jax.random.randint(jax.random.fold_in(_rk, 7), (8,), 0, max(1, 256 // 4) + 1, jnp.int32)
        _lenS2 = 256 - jax.random.randint(jax.random.fold_in(_rk, 8), (8,), 0, max(1, 256 // 4) + 1, jnp.int32)
        condB_coeff = 0.00219231 + 0.0100837 * jax.random.normal(jax.random.fold_in(_rk, 11), (8,), jnp.float32)
        itok_B_0_23 = jax.random.randint(jax.random.fold_in(_rk, 13), (8,), 0, 24, jnp.int32)
        _validS = jnp.arange(256)[None, :] < _lenS[:, None]
        _validS2 = jnp.arange(256)[None, :] < _lenS2[:, None]
        _causal = jnp.tril(jnp.ones((256, 256), dtype=bool))
        mask_Bx4096x4096_ik1 = jnp.where(jnp.ones((8, 1024, 1024), dtype=bool), 1, 0).astype(jnp.int32)
        return (x, condB_coeff, itok_B_0_23, mask_Bx4096x4096_ik1)
    x, condB_coeff, itok_B_0_23, mask_Bx4096x4096_ik1 = _rec_inputs()

    def _L0_cond_setup():
        import jax, jax.numpy as jnp
        import numpy as np
        B, S, D_IN, D_OUT = (4, 128, 1024, 1024)
        key = jax.random.key(seed)
        k1, k2, k3, k4, k5 = jax.random.split(key, 5)
        hidden_states = jax.random.normal(k1, (B, S, D_IN), dtype=jnp.float32)
        W = jax.random.normal(k2, (D_OUT, D_IN), dtype=jnp.float32) * 0.02
        b = jax.random.normal(k3, (D_OUT,), dtype=jnp.float32) * 0.02
        coeff = jax.random.normal(k4, (B,), dtype=jnp.float32) * 0.01
        mask = jax.random.randint(k5, (B, D_IN, D_OUT), 0, 2, dtype=jnp.int32)
        return {'hidden_states': hidden_states, 'W': W, 'b': b, 'coeff': coeff, 'mask': mask}
    _L0_cond_all = _L0_cond_setup()
    _L0_cond_in = {k: v for k, v in _L0_cond_all.items() if k in ('W', 'b')}
    del _L0_cond_all

    def _L1_cond_setup():
        import jax, jax.numpy as jnp
        import numpy as np
        R = 16
        ALPHA = 32
        SCALING = ALPHA / R
        SLOTS = 32
        IN_F = 1024
        OUT_F = 1024
        B, T = (8, 256)
        key = jax.random.key(seed)
        k1, k2, k3, k4, k5, k6 = jax.random.split(key, 6)
        x = jax.random.normal(k1, (B, T, IN_F), dtype=jnp.float32)
        adapter_mapping = jax.random.randint(k2, (B,), 0, SLOTS, dtype=jnp.int32)
        W = jax.random.normal(k3, (OUT_F, IN_F), dtype=jnp.float32) * 0.02
        b = jax.random.normal(k4, (OUT_F,), dtype=jnp.float32) * 0.02
        lora_As = jax.random.normal(k5, (SLOTS, IN_F, R), dtype=jnp.float32) * 0.02
        lora_Bs = jax.random.normal(k6, (SLOTS, R, OUT_F), dtype=jnp.float32) * 0.02
        return {'x': x, 'adapter_mapping': adapter_mapping, 'W': W, 'b': b, 'lora_As': lora_As, 'lora_Bs': lora_Bs}
    _L1_cond_all = _L1_cond_setup()
    _L1_cond_in = {k: v for k, v in _L1_cond_all.items() if k in ('W', 'b', 'lora_As', 'lora_Bs')}
    del _L1_cond_all
    return {'x': x, 'condB_coeff': condB_coeff, 'itok_B_0_23': itok_B_0_23, 'mask_Bx4096x4096_ik1': mask_Bx4096x4096_ik1, 'L0_cond_W': _L0_cond_in['W'], 'L0_cond_b': _L0_cond_in['b'], 'L1_cond_W': _L1_cond_in['W'], 'L1_cond_b': _L1_cond_in['b'], 'L1_cond_lora_As': _L1_cond_in['lora_As'], 'L1_cond_lora_Bs': _L1_cond_in['lora_Bs']}

def reference(x, condB_coeff, itok_B_0_23, mask_Bx4096x4096_ik1, L0_cond_W, L0_cond_b, L1_cond_W, L1_cond_b, L1_cond_lora_As, L1_cond_lora_Bs):
    import jax
    import jax.numpy as jnp

    def _L0_cond_ref(hidden_states, W, b, coeff, mask):
        import jax, jax.numpy as jnp
        import numpy as np
        B, S, D_IN, D_OUT = (4, 128, 1024, 1024)
        output = jnp.einsum('bsi,oi->bso', hidden_states, W) + b
        sign = (2 * mask - 1).astype(hidden_states.dtype)
        diff = jnp.einsum('bsi,bio->bso', hidden_states, sign)
        return output + diff * coeff[:, None, None]

    def _L1_cond_ref(x, adapter_mapping, W, b, lora_As, lora_Bs):
        import jax, jax.numpy as jnp
        import numpy as np
        R = 16
        ALPHA = 32
        SCALING = ALPHA / R
        SLOTS = 32
        IN_F = 1024
        OUT_F = 1024
        B, T = (8, 256)
        base_out = jnp.einsum('bti,oi->bto', x, W) + b
        A = lora_As[adapter_mapping]
        Bm = lora_Bs[adapter_mapping]
        lora_h = jnp.einsum('bti,bir->btr', x, A)
        lora_out = jnp.einsum('btr,bro->bto', lora_h, Bm)
        return base_out + lora_out * SCALING
    x = x + _L0_cond_ref(x, L0_cond_W, L0_cond_b, condB_coeff, mask_Bx4096x4096_ik1)
    x = x + _L1_cond_ref(x, itok_B_0_23, L1_cond_W, L1_cond_b, L1_cond_lora_As, L1_cond_lora_Bs)
    return x

_drawn_inputs = setup_inputs


def setup_inputs(seed=0):
    import zlib

    import numpy as np

    out = dict(_drawn_inputs(seed))
    spreads = {}
    factors = {'L0_cond_b': 3.411, 'L1_cond_b': 4.716}
    for name, (base, spread) in spreads.items():
        noise = np.random.default_rng([zlib.crc32(name.encode()), seed]).standard_normal(out[name].shape)
        drawn = base * np.exp(spread * noise) if base else spread * noise
        out[name] = jnp.asarray(drawn.astype(out[name].dtype))
    for name, factor in factors.items():
        out[name] = (out[name] * factor).astype(out[name].dtype)
    return out
```

```python
from contextlib import ExitStack

import concourse.bass as bass
from concourse import mybir

ALU = mybir.AluOpType
ACT = mybir.ActivationFunctionType
F32 = mybir.dt.float32
F32R = mybir.dt.float32r
I32 = mybir.dt.int32

P = 128
BANK = 512
RING = 4
SCALING = 2.0


def cond_residual_two_layers(nc, x, coeff, slot_ids, mask, w0, b0, w1, b1, lora_a, lora_b, out):
    NB, T, D = x.shape
    SLOTS, _, R = lora_a.shape
    KT = D // P
    ST = T // P
    NH = D // BANK
    PAIR = BANK // T
    XG = KT // PAIR
    OG = ST * NH
    WCH = 4
    WG = 2 * KT
    W0C = D // WCH
    LR = 3 * 2 * R
    KS = LR + 2
    assert PAIR == 2 and ST == 2 and NH == 2 and XG == 4 and OG == 4 and LR == 96

    with ExitStack() as ctx:
        def sb(name, shape, dt):
            return ctx.enter_context(nc.sbuf_tensor(name, shape, dt))

        def sem(name):
            return ctx.enter_context(nc.semaphore(name))

        ident = sb("ident", [P, P], F32)
        coeff_all = sb("coeff_all", [P, NB], F32)
        coeff_pairs = sb("coeff_pairs", [P, NB, 2], F32)
        coeff_now = sb("coeff_now", [P, 2], F32)
        ids = sb("ids", [1, NB], I32)
        b0_rows = sb("b0_rows", [KT, P], F32)
        b0_cols = sb("b0_cols", [P, KT], F32)
        w_stage = sb("w_stage", [P, 2, D * W0C // P], F32)
        w0_t = sb("w0_t", [P, KT, D], F32)
        w1_hi = sb("w1_hi", [P, KT, D], F32R)
        w1_lo = sb("w1_lo", [P, KT, D], F32R)
        masks = sb("masks", [P, RING, D], I32)
        sums = masks[:].bitcast(F32)
        wc_hi = sb("wc_hi", [P, RING, D], F32R)
        wc_lo = sb("wc_lo", [P, RING, D], F32R)
        x_rows = sb("x_rows", [P, ST, D], F32)
        x_hi = sb("x_hi", [P, KT, T], F32R)
        x_lo = sb("x_lo", [P, KT, T], F32R)
        y_hi = sb("y_hi", [P, KT, T], F32R)
        y_lo = sb("y_lo", [P, KT, T], F32R)
        a_raw = sb("a_raw", [P, KT, R], F32)
        a_parts = sb("a_parts", [P, KT, 3, 2 * R], F32R)
        b_raw = sb("b_raw", [P, D], F32)
        b_stack = sb("b_stack", [P, D], F32R)
        h_stack = sb("h_stack", [P, T], F32R)
        z_rows = sb("z_rows", [P, OG, BANK], F32)

        y_ps = [ctx.enter_context(nc.psum_tensor(f"y_ps{j}", [P, BANK], F32)) for j in range(XG)]
        z_ps = [ctx.enter_context(nc.psum_tensor(f"z_ps{j}", [P, BANK], F32)) for j in range(2)]
        t_ps = [ctx.enter_context(nc.psum_tensor(f"t_ps{j}", [P, BANK], F32)) for j in range(2)]

        consts_in = sem("consts_in")
        ids_in = sem("ids_in")
        b1_in = sem("b1_in")
        x_in = sem("x_in")
        w_in = [sem(f"w_in{j}") for j in range(2)]
        mask_in = [sem(f"mask_in{j}") for j in range(RING)]
        lora_in = sem("lora_in")
        z_out = [sem(f"z_out{g}") for g in range(OG)]
        ident_zero = sem("ident_zero")
        ident_done = sem("ident_done")
        pairs_done = sem("pairs_done")
        b1_done = sem("b1_done")
        ones_done = sem("ones_done")
        diag_done = sem("diag_done")
        lora_hi_done = sem("lora_hi_done")
        lora_lo_done = sem("lora_lo_done")
        b0_ps = sem("b0_ps")
        b0_done = sem("b0_done")
        wt_ps = sem("wt_ps")
        w0_done = sem("w0_done")
        w1_hi_done = sem("w1_hi_done")
        w1_lo_done = sem("w1_lo_done")
        xt_ps = sem("xt_ps")
        x_hi_done = sem("x_hi_done")
        x_lo_done = sem("x_lo_done")
        coeff_set = sem("coeff_set")
        signed_done = sem("signed_done")
        sum_done = sem("sum_done")
        wc_hi_done = sem("wc_hi_done")
        wc_lo_done = sem("wc_lo_done")
        block_used = sem("block_used")
        y_full = sem("y_full")
        y_hi_done = sem("y_hi_done")
        y_lo_done = sem("y_lo_done")
        h_full = sem("h_full")
        h_hi_done = sem("h_hi_done")
        h_lo_done = sem("h_lo_done")
        z_full = sem("z_full")
        z_done = sem("z_done")

        x_v = x.rearrange("b (s p) d -> b p s d", p=P)
        mask_v = mask.rearrange("b (k p) o -> b k p o", p=P)
        out_v = out.rearrange("b (s p) (h n) -> b s h p n", p=P, n=BANK)
        w0_v = w0.rearrange("(a p) (q c) -> q p a c", p=P, c=W0C)
        w1_v = w1.rearrange("(h a p) (q c) -> h q p a c", p=P, h=NH, c=BANK)
        la_v = lora_a.rearrange("s (k p) r -> s p k r", p=P)
        w_stage0 = w_stage[:].rearrange("p j (a c) -> p j a c", c=W0C)
        w_stage1 = w_stage[:].rearrange("p j (a c) -> p j a c", c=BANK)

        def need(eng, s, n):
            if not (isinstance(n, int) and n <= 0):
                eng.wait_ge(s, n)

        def block_read(eng, b, k):
            if k < 0:
                b, k = b - 1, k + KT
            if isinstance(b, int) and b < 0:
                return
            if k == KT - 1:
                eng.wait_ge(y_full, XG * b + XG)
            else:
                eng.wait_ge(block_used, (KT - 1) * b + k + 1)

        block = ctx.enter_context(nc.Block())

        @block.sync
        def _(sp):
            def load_x(b):
                need(sp, xt_ps, XG * b)
                sp.dma_start(x_rows[:], x_v[bass.ds(b, 1)].rearrange("a p s d -> (a p) s d")).then_inc(x_in, 16)

            def load_mask(b, k):
                need(sp, wc_lo_done, KT * b + k - RING + 1)
                sp.dma_start(masks[:, k % RING, :],
                             mask_v[bass.ds(b, 1), k].rearrange("a p o -> (a p) o")).then_inc(mask_in[k % RING], 16)

            def load_weight(j):
                need(sp, wt_ps, 4 * (j - 1))
                if j < WCH:
                    sp.dma_start(w_stage0[:, j % 2], w0_v[j]).then_inc(w_in[j % 2], 16)
                else:
                    h, q = divmod(j - WCH, 2)
                    sp.dma_start(w_stage1[:, j % 2], w1_v[h, q]).then_inc(w_in[j % 2], 16)

            def load_lora(b):
                slot = sp.value_load(ids[0:1, bass.ds(b, 1)], min_val=0, max_val=SLOTS - 1)
                need(sp, lora_lo_done, 4 * b)
                sp.dma_start(a_raw[:], la_v[bass.ds(slot, 1)].rearrange("a p k r -> (a p) k r")).then_inc(lora_in, 16)
                for j in range(6):
                    sp.dma_start(b_raw[j * R:(j + 1) * R, :],
                                 lora_b[bass.ds(slot, 1)].rearrange("a r o -> (a r) o")).then_inc(lora_in, 16)

            sp.dma_start(x_rows[:], x_v[0]).then_inc(x_in, 16)
            load_weight(0)
            sp.dma_start(coeff_all[:], coeff.rearrange("(a n) -> a n", a=1).to_broadcast([P, NB])).then_inc(consts_in, 16)
            sp.dma_start(b0_rows[:], b0.rearrange("(k p) -> k p", p=P)).then_inc(consts_in, 16)
            sp.dma_start(ids[:], slot_ids.rearrange("(a n) -> a n", a=1)).then_inc(ids_in, 16)
            for j in range(2):
                sp.dma_start(b_raw[LR + j:LR + j + 1, :], b1.rearrange("(a n) -> a n", a=1)).then_inc(b1_in, 16)
            load_mask(0, 0)
            load_weight(1)
            for k in range(1, 4):
                load_mask(0, k)
            load_weight(2)
            load_mask(0, 4)
            load_weight(3)
            for k in range(5, KT):
                load_mask(0, k)
            load_weight(4)
            load_weight(5)
            sp.wait_ge(ids_in, 16)
            load_lora(0)
            load_x(1)
            load_weight(6)
            load_mask(1, 0)
            load_weight(7)
            for k in range(1, KT):
                load_mask(1, k)
            with sp.Fori(1, NB - 1) as b:
                load_lora(b)
                load_x(b + 1)
                for k in range(KT):
                    load_mask(b + 1, k)
            load_lora(NB - 1)

        @block.gpsimd
        def _(pool):
            pool.memset(ident[:], 0.0).then_inc(ident_zero, 1)
            pool.wait_ge(ident_zero, 1)
            pool.affine_select(out=ident[:], in_=ident[:], compare_op=ALU.not_equal, fill=1.0, base=0,
                               pattern=[[-1, P]], channel_multiplier=1).then_inc(ident_done, 1)
            pool.wait_ge(consts_in, 32)
            pool.tensor_scalar(coeff_pairs[:, :, 0], coeff_all[:], 2.0, None, ALU.mult).then_inc(pairs_done, 1)
            pool.tensor_scalar(coeff_pairs[:, :, 1], coeff_all[:], -1.0, None, ALU.mult).then_inc(pairs_done, 1)
            pool.wait_ge(ident_done, 1)

            def raise_diagonal(j):
                need(pool, w_in[j % 2], 16 * (j // 2 + 1))
                if j < WCH:
                    per = W0C // P
                    blocks = [w_stage0[:, j % 2, j * per + n, n * P:(n + 1) * P] for n in range(per)]
                else:
                    h, q = divmod(j - WCH, 2)
                    blocks = [w_stage1[:, j % 2, n, n * P:(n + 1) * P] for n in range(BANK // P)] if h == q else []
                for blk in blocks:
                    pool.tensor_tensor(blk, blk, ident[:], ALU.add).then_inc(diag_done, 1)

            for j in range(WCH):
                raise_diagonal(j)
            pool.wait_ge(diag_done, 8)
            pool.wait_ge(b1_in, 32)
            pool.tensor_copy(b_stack[LR:KS, :], b_raw[LR:KS, :]).then_inc(b1_done, 1)
            pool.wait_ge(b1_done, 1)
            pool.tensor_tensor(b_stack[LR:KS, :], b_raw[LR:KS, :], b_stack[LR:KS, :].bitcast(F32),
                               ALU.subtract).then_inc(b1_done, 1)
            pool.wait_ge(b1_done, 2)
            pool.tensor_copy(b_stack[LR:LR + 1, :], b_raw[LR:LR + 1, :]).then_inc(b1_done, 1)
            pool.wait_ge(b1_done, 3)
            for j in range(WCH, 2 * WCH):
                raise_diagonal(j)

            def lora_low(b):
                pool.wait_ge(lora_hi_done, 4 * (b + 1))
                for n in range(3):
                    pool.tensor_tensor(a_parts[:, :, n, R:2 * R], a_raw[:],
                                       a_parts[:, :, n, 0:R].bitcast(F32), ALU.subtract).then_inc(lora_lo_done, 1)
                pool.wait_ge(lora_lo_done, 4 * b + 3)
                pool.tensor_tensor(b_stack[4 * R:LR, :], b_raw[4 * R:LR, :],
                                   b_stack[4 * R:LR, :].bitcast(F32), ALU.subtract).then_inc(lora_lo_done, 1)

            with pool.Fori(0, NB) as b:
                lora_low(b)

        @block.tensor
        def _(pe):
            def weight_group(j):
                c, g = divmod(j, 4)
                if g == 0:
                    pe.wait_ge(w_in[c % 2], 16 * (c // 2 + 1))
                    diagonals = [2, 4, 6, 8, 12, 12, 12, 16][c]
                    pe.wait_ge(diag_done, diagonals)
                if c < WCH:
                    src = [w_stage0[:, c % 2, (g % 2) * 4 + n, (g // 2) * P:(g // 2 + 1) * P] for n in range(4)]
                    need(pe, w0_done, j - 1)
                else:
                    src = [w_stage1[:, c % 2, n, g * P:(g + 1) * P] for n in range(4)]
                    if j < WG + 2:
                        pe.wait_ge(w0_done, j - 1)
                    elif 3 * WG // 2 <= j < 3 * WG // 2 + 2:
                        pe.wait_ge(z_done, j - 3 * WG // 2 + 1)
                    else:
                        pe.wait_ge(w1_lo_done, j - WG - 1)
                for n in range(4):
                    ins = pe.transpose(z_ps[j % 2][:, n * P:(n + 1) * P], src[n], ident[:])
                ins.then_inc(wt_ps, 1)

            def x_group(b, g):
                if g == 0:
                    pe.wait_ge(x_in, 16 * (b + 1))
                if g == 2:
                    pe.wait_ge(x_lo_done, XG * b + 2)
                if g == 3:
                    pe.wait_ge(x_lo_done, XG * b + 1)
                    need(pe, h_lo_done, b)
                bank = t_ps[(0, 1, 1, 0)[g]]
                for n in range(PAIR):
                    for s in range(ST):
                        ins = pe.transpose(bank[:, n * T + s * P:n * T + (s + 1) * P],
                                           x_rows[:, s, (PAIR * g + n) * P:(PAIR * g + n + 1) * P], ident[:])
                ins.then_inc(xt_ps, 1)

            def layer0_block(b, k):
                if k == 0:
                    pe.wait_ge(x_lo_done, XG * (b + 1))
                    need(pe, y_lo_done, KT * b)
                pe.wait_ge(wc_lo_done, KT * b + k + 1)
                for o in range(KT):
                    acc = y_ps[o // PAIR][:, (o % PAIR) * T:(o % PAIR + 1) * T]
                    for n, (w, xs) in enumerate(((wc_hi, x_hi), (wc_hi, x_lo), (wc_lo, x_hi))):
                        ins = pe.matmul(acc, w[:, k % RING, o * P:(o + 1) * P], xs[:, k, :],
                                        start=(k == 0 and o % PAIR == 0 and n == 0),
                                        stop=(k == KT - 1 and n == 2), skip_group_check=True)
                    if k == KT - 1 and o % PAIR == PAIR - 1:
                        ins.then_inc(y_full, 1)
                if k < KT - 1:
                    ins.then_inc(block_used, 1)

            def layer1_group(b, g, first=False):
                s, h = g % ST, g // ST
                if g == 0 and first:
                    pe.wait_ge(w1_lo_done, WG // 2)
                if g == 2 and first:
                    pe.wait_ge(w1_lo_done, WG)
                need(pe, z_done, OG * b + g - 1)
                for k in range(KT):
                    if g == 0:
                        pe.wait_ge(y_lo_done, KT * b + k + 1)
                    for n, (ys, w) in enumerate(((y_hi, w1_hi), (y_hi, w1_lo), (y_lo, w1_hi))):
                        pe.matmul(z_ps[g % 2][:], ys[:, k, s * P:(s + 1) * P], w[:, k, h * BANK:(h + 1) * BANK],
                                  start=(k == 0 and n == 0), stop=False)

            def lora_hidden(b, first, last):
                if first:
                    pe.wait_ge(ones_done, 1)
                    pe.wait_ge(b1_done, 3)
                pe.wait_ge(lora_lo_done, 4 * (b + 1))
                if not last:
                    pe.wait_ge(x_lo_done, XG * (b + 1) + 1)
                for k in range(KT):
                    for n, ys in enumerate((y_hi, y_lo)):
                        ins = pe.matmul(t_ps[0][0:LR, 0:T], a_parts[:, k].rearrange("p n r -> p (n r)"), ys[:, k, :],
                                        start=(k == 0 and n == 0), stop=(k == KT - 1 and n == 1))
                ins.then_inc(h_full, 1)

            def close_group(b, g):
                s, h = g % ST, g // ST
                if g == 0:
                    pe.wait_ge(h_lo_done, b + 1)
                    pe.wait_ge(h_hi_done, b + 1)
                pe.matmul(z_ps[g % 2][:], h_stack[0:KS, s * P:(s + 1) * P], b_stack[0:KS, h * BANK:(h + 1) * BANK],
                          start=False, stop=True).then_inc(z_full, 1)

            def batch(b, first=False, last=False):
                for k in range(KT):
                    layer0_block(b, k)
                    if first:
                        for j in {1: range(8, 12), 3: range(12, 16), 5: range(16, 20), 6: range(20, 24)}.get(k, ()):
                            weight_group(j)
                if not last:
                    x_group(b + 1, 0)
                    x_group(b + 1, 1)
                layer1_group(b, 0, first)
                lora_hidden(b, first, last)
                layer1_group(b, 1)
                close_group(b, 0)
                if not last:
                    x_group(b + 1, 2)
                close_group(b, 1)
                if not last:
                    x_group(b + 1, 3)
                if first:
                    for j in range(24, 32):
                        weight_group(j)
                for g in (2, 3):
                    layer1_group(b, g, first)
                    close_group(b, g)

            pe.wait_ge(ident_done, 1)
            pe.wait_ge(consts_in, 32)
            pe.transpose(y_ps[0][:, 0:KT], b0_rows[:], ident[0:KT, 0:KT]).then_inc(b0_ps, 1)
            for g in range(XG):
                x_group(0, g)
            for j in range(8):
                weight_group(j)
            pe.wait_ge(b0_done, 1)
            batch(0, first=True)
            with pe.Fori(1, NB - 1) as b:
                batch(b)
            batch(NB - 1, last=True)

        @block.scalar
        def _(act):
            def set_coeff(b):
                need(act, signed_done, KT * b)
                act.activation(coeff_now[:], coeff_pairs[:, bass.ds(b, 1), :].rearrange("p a n -> p (a n)"),
                               ACT.Copy).then_inc(coeff_set, 1)
                act.wait_ge(coeff_set, b + 1)

            def signed_mask(b, k):
                act.wait_ge(mask_in[k % RING], 16 * (2 * b + k // RING + 1))
                act.activation(sums[:, k % RING, :], masks[:, k % RING, :], ACT.Identity,
                               bias=coeff_now[:, 1:2], scale=coeff_now[:, 0:1]).then_inc(signed_done, 1)

            def weights_high(b, k):
                act.wait_ge(sum_done, KT * b + k + 1)
                block_read(act, b, k - RING)
                act.activation(wc_hi[:, k % RING, :], sums[:, k % RING, :], ACT.Copy).then_inc(wc_hi_done, 1)

            def step(b, k, more=True):
                if k < KT - 1:
                    signed_mask(b, k + 1)
                elif more:
                    set_coeff(b + 1)
                    signed_mask(b + 1, 0)
                weights_high(b, k)

            def x_high(b, g):
                act.wait_ge(xt_ps, XG * b + g + 1)
                act.activation(x_hi[:, PAIR * g:PAIR * (g + 1), :], t_ps[(0, 1, 1, 0)[g]][:].rearrange(
                    "p (n t) -> p n t", n=PAIR), ACT.Copy).then_inc(x_hi_done, 1)

            def weight_copy(j):
                act.wait_ge(wt_ps, j + 1)
                if j < WG:
                    k, h = divmod(j, 2)
                    act.activation(w0_t[:, k, h * BANK:(h + 1) * BANK], z_ps[j % 2][:], ACT.Copy).then_inc(w0_done, 1)
                else:
                    h, k = divmod(j - WG, KT)
                    act.activation(w1_hi[:, k, h * BANK:(h + 1) * BANK], z_ps[j % 2][:],
                                   ACT.Copy).then_inc(w1_hi_done, 1)

            def y_high(b, g):
                act.wait_ge(y_full, XG * b + g + 1)
                for o in range(PAIR * g, PAIR * (g + 1)):
                    act.activation(y_hi[:, o, :], y_ps[g][:, (o % PAIR) * T:(o % PAIR + 1) * T], ACT.Identity,
                                   bias=b0_cols[:, o:o + 1]).then_inc(y_hi_done, 1)

            def h_high(b):
                act.wait_ge(h_full, b + 1)
                act.activation(h_stack[0:LR, :], t_ps[0][0:LR, 0:T], ACT.Copy, scale=SCALING).then_inc(h_hi_done, 1)

            def z_copy(b, g):
                act.wait_ge(z_full, OG * b + g + 1)
                need(act, z_out[g], 16 * b)
                act.activation(z_rows[:, g, :], z_ps[g % 2][:], ACT.Copy).then_inc(z_done, 1)

            def store(b, g):
                s, h = g % ST, g // ST
                act.wait_ge(z_done, OG * b + g + 1)
                act.dma_start(out_v[bass.ds(b, 1), s, h].rearrange("a p n -> (a p) n"),
                              z_rows[:, g, :]).then_inc(z_out[g], 16)

            def lora_high(b):
                act.wait_ge(lora_in, 16 * 7 * (b + 1))
                need(act, z_full, OG * b)
                for n in range(3):
                    act.activation(a_parts[:, :, n, 0:R], a_raw[:], ACT.Copy).then_inc(lora_hi_done, 1)
                act.activation(b_stack[0:LR, :], b_raw[0:LR, :], ACT.Copy).then_inc(lora_hi_done, 1)

            def batch(b, first=False, last=False):
                for k in range(RING, KT):
                    if first:
                        for j in {4: range(8, 12), 6: range(12, 16), 7: range(16, 20)}.get(k, ()):
                            weight_copy(j)
                    step(b, k, not last)
                    if k == RING + 1 and not first:
                        lora_high(b)
                if first:
                    for j in range(20, 24):
                        weight_copy(j)
                    lora_high(b)
                for g in range(XG):
                    y_high(b, g)
                if not last:
                    x_high(b + 1, 0)
                    x_high(b + 1, 1)
                    step(b + 1, 0)
                    step(b + 1, 1)
                h_high(b)
                if not last:
                    step(b + 1, 2)
                z_copy(b, 0)
                if not last:
                    x_high(b + 1, 2)
                store(b, 0)
                z_copy(b, 1)
                if not last:
                    x_high(b + 1, 3)
                store(b, 1)
                if first:
                    for j in range(24, 32):
                        weight_copy(j)
                if not last:
                    step(b + 1, 3)
                for g in (2, 3):
                    z_copy(b, g)
                    store(b, g)

            act.wait_ge(pairs_done, 2)
            set_coeff(0)
            act.wait_ge(b0_ps, 1)
            act.activation(b0_cols[:], y_ps[0][:, 0:KT], ACT.Copy).then_inc(b0_done, 1)
            for g in range(XG):
                x_high(0, g)
            act.wait_ge(b0_done, 1)
            signed_mask(0, 0)
            for j in range(4):
                weight_copy(j)
            step(0, 0)
            for j in range(4, 8):
                weight_copy(j)
            for k in range(1, RING):
                step(0, k)
            batch(0, first=True)
            with act.Fori(1, NB - 1) as b:
                batch(b)
            batch(NB - 1, last=True)
            for g in range(OG):
                act.wait_ge(z_out[g], 16 * NB)

        @block.vector
        def _(dve):
            def weights_sum(b, k):
                dve.wait_ge(signed_done, KT * b + k + 1)
                if isinstance(b, int) and b == 0:
                    dve.wait_ge(w0_done, 2 * (k + 1))
                dve.tensor_tensor(sums[:, k % RING, :], sums[:, k % RING, :], w0_t[:, k, :],
                                  ALU.add).then_inc(sum_done, 1)

            def weights_low(b, k):
                dve.wait_ge(wc_hi_done, KT * b + k + 1)
                dve.wait_ge(sum_done, KT * b + k + 1)
                dve.tensor_tensor(wc_lo[:, k % RING, :], sums[:, k % RING, :],
                                  wc_hi[:, k % RING, :].bitcast(F32), ALU.subtract).then_inc(wc_lo_done, 1)

            def step(b, k, more=True):
                if k < KT - 1:
                    weights_sum(b, k + 1)
                elif more:
                    weights_sum(b + 1, 0)
                weights_low(b, k)

            def x_low(b, g):
                dve.wait_ge(x_hi_done, XG * b + g + 1)
                dve.tensor_tensor(x_lo[:, PAIR * g:PAIR * (g + 1), :],
                                  t_ps[(0, 1, 1, 0)[g]][:].rearrange("p (n t) -> p n t", n=PAIR),
                                  x_hi[:, PAIR * g:PAIR * (g + 1), :].bitcast(F32),
                                  ALU.subtract).then_inc(x_lo_done, 1)

            def w1_low(j):
                dve.wait_ge(w1_hi_done, j - WG + 1)
                h, k = divmod(j - WG, KT)
                dve.tensor_tensor(w1_lo[:, k, h * BANK:(h + 1) * BANK], z_ps[j % 2][:],
                                  w1_hi[:, k, h * BANK:(h + 1) * BANK].bitcast(F32),
                                  ALU.subtract).then_inc(w1_lo_done, 1)

            def y_low(b, g):
                dve.wait_ge(y_hi_done, KT * b + PAIR * (g + 1))
                for o in range(PAIR * g, PAIR * (g + 1)):
                    dve.scalar_tensor_tensor(out=y_lo[:, o, :], in0=y_ps[g][:, (o % PAIR) * T:(o % PAIR + 1) * T],
                                             scalar=b0_cols[:, o:o + 1], in1=y_hi[:, o, :].bitcast(F32),
                                             op0=ALU.add, op1=ALU.subtract).then_inc(y_lo_done, 1)

            def h_low(b):
                dve.wait_ge(h_hi_done, b + 1)
                dve.scalar_tensor_tensor(out=h_stack[2 * R:4 * R, :], in0=t_ps[0][2 * R:4 * R, 0:T], scalar=SCALING,
                                         in1=h_stack[2 * R:4 * R, :].bitcast(F32),
                                         op0=ALU.mult, op1=ALU.subtract).then_inc(h_lo_done, 1)

            def batch(b, first=False, last=False):
                for k in range(RING, KT):
                    if first and k >= 6:
                        for j in {6: range(16, 16), 7: range(16, 20)}[k]:
                            w1_low(j)
                    step(b, k, not last)
                if first:
                    for j in range(20, 24):
                        w1_low(j)
                for g in range(XG):
                    y_low(b, g)
                if not last:
                    x_low(b + 1, 0)
                    x_low(b + 1, 1)
                    step(b + 1, 0)
                    step(b + 1, 1)
                h_low(b)
                if not last:
                    step(b + 1, 2)
                    x_low(b + 1, 2)
                    x_low(b + 1, 3)
                if first:
                    for j in range(24, 32):
                        w1_low(j)
                if not last:
                    step(b + 1, 3)

            dve.memset(h_stack[LR:P, :].bitcast(F32), 1.0).then_inc(ones_done, 1)
            for g in range(XG):
                x_low(0, g)
            weights_sum(0, 0)
            for k in range(RING):
                step(0, k)
            dve.wait_ge(b0_done, 1)
            batch(0, first=True)
            with dve.Fori(1, NB - 1) as b:
                batch(b)
            batch(NB - 1, last=True)


def kernel(x, condB_coeff, itok_B_0_23, mask_Bx4096x4096_ik1, L0_cond_W, L0_cond_b, L1_cond_W, L1_cond_b,
           L1_cond_lora_As, L1_cond_lora_Bs):
    import numpy as np
    import concourse.bacc as bacc
    from concourse.bass_utils import run_bass_kernel_spmd

    nc = bacc.Bacc("TRN2", target_bir_lowering=False, num_devices=1, dynamic_dma_scratch_size=1024)
    given = {"x": x, "coeff": condB_coeff, "slot_ids": itok_B_0_23, "mask": mask_Bx4096x4096_ik1,
             "w0": L0_cond_W, "b0": L0_cond_b, "w1": L1_cond_W, "b1": L1_cond_b,
             "lora_a": L1_cond_lora_As, "lora_b": L1_cond_lora_Bs}
    arrays, args = {}, []
    for name, a in given.items():
        a = np.ascontiguousarray(a)
        arrays[f"in_{name}"] = a
        args.append(nc.dram_tensor(f"in_{name}", a.shape, mybir.dt.from_np(a.dtype), kind="ExternalInput").ap())
    args.append(nc.dram_tensor("out", arrays["in_x"].shape, F32, kind="ExternalOutput").ap())
    cond_residual_two_layers(nc, *args)
    result = run_bass_kernel_spmd(nc, [arrays], core_ids=[0])
    return result.results[0]["out"]
```

```python
from contextlib import ExitStack

import concourse.bass as bass
from concourse import mybir

ALU = mybir.AluOpType
ACT = mybir.ActivationFunctionType
F32 = mybir.dt.float32
F32R = mybir.dt.float32r
I32 = mybir.dt.int32

P = 128
BANK = 512
RING = 4
SCALING = 2.0


def cond_residual_two_layers(nc, x, coeff, slot_ids, mask, w0, b0, w1, b1, lora_a, lora_b, out):
    NB, T, D = x.shape
    SLOTS, _, R = lora_a.shape
    KT = D // P
    ST = T // P
    NH = D // BANK
    PAIR = BANK // T
    XG = KT // PAIR
    OG = ST * NH
    WCH = 4
    WG = 2 * KT
    W0C = D // WCH
    LR = 3 * 2 * R
    KS = LR + 2
    assert PAIR == 2 and ST == 2 and NH == 2 and XG == 4 and OG == 4 and LR == 96

    with ExitStack() as ctx:
        def sb(name, shape, dt):
            return ctx.enter_context(nc.sbuf_tensor(name, shape, dt))

        def sem(name):
            return ctx.enter_context(nc.semaphore(name))

        ident = sb("ident", [P, P], F32)
        coeff_all = sb("coeff_all", [P, NB], F32)
        coeff_pairs = sb("coeff_pairs", [P, NB, 2], F32)
        coeff_now = sb("coeff_now", [P, 2], F32)
        ids = sb("ids", [1, NB], I32)
        b0_rows = sb("b0_rows", [KT, P], F32)
        b0_cols = sb("b0_cols", [P, KT], F32)
        w_stage = sb("w_stage", [P, 2, D * W0C // P], F32)
        w0_t = sb("w0_t", [P, KT, D], F32)
        w1_hi = sb("w1_hi", [P, KT, D], F32R)
        w1_lo = sb("w1_lo", [P, KT, D], F32R)
        masks = sb("masks", [P, RING, D], I32)
        sums = masks[:].bitcast(F32)
        wc_hi = sb("wc_hi", [P, RING, D], F32R)
        wc_lo = sb("wc_lo", [P, RING, D], F32R)
        x_rows = sb("x_rows", [P, ST, D], F32)
        x_hi = sb("x_hi", [P, KT, T], F32R)
        x_lo = sb("x_lo", [P, KT, T], F32R)
        y_hi = sb("y_hi", [P, KT, T], F32R)
        y_lo = sb("y_lo", [P, KT, T], F32R)
        a_raw = sb("a_raw", [P, KT, R], F32)
        a_parts = sb("a_parts", [P, KT, 3, 2 * R], F32R)
        b_raw = sb("b_raw", [P, D], F32)
        b_stack = sb("b_stack", [P, D], F32R)
        h_stack = sb("h_stack", [P, T], F32R)
        z_rows = sb("z_rows", [P, OG, BANK], F32)

        y_ps = [ctx.enter_context(nc.psum_tensor(f"y_ps{j}", [P, BANK], F32)) for j in range(XG)]
        z_ps = [ctx.enter_context(nc.psum_tensor(f"z_ps{j}", [P, BANK], F32)) for j in range(2)]
        t_ps = [ctx.enter_context(nc.psum_tensor(f"t_ps{j}", [P, BANK], F32)) for j in range(2)]

        consts_in = sem("consts_in")
        ids_in = sem("ids_in")
        b1_in = sem("b1_in")
        x_half_in = [sem(f"x_half_in{j}") for j in range(2)]
        x_in = sem("x_in")
        w_in = [sem(f"w_in{j}") for j in range(3)]
        mask_in = [sem(f"mask_in{j}") for j in range(RING)]
        lora_in = sem("lora_in")
        z_out = [sem(f"z_out{g}") for g in range(OG)]
        ident_zero = sem("ident_zero")
        ident_done = sem("ident_done")
        pairs_done = sem("pairs_done")
        b1_done = sem("b1_done")
        ones_done = sem("ones_done")
        diag_done = sem("diag_done")
        lora_hi_done = sem("lora_hi_done")
        lora_lo_done = sem("lora_lo_done")
        b0_ps = sem("b0_ps")
        b0_done = sem("b0_done")
        wt_ps = sem("wt_ps")
        w0_left = sem("w0_left")
        w0_right = sem("w0_right")
        w1_hi_done = sem("w1_hi_done")
        w1_lo_done = sem("w1_lo_done")
        xt_ps = sem("xt_ps")
        x_hi_done = sem("x_hi_done")
        x_lo_done = sem("x_lo_done")
        coeff_set = sem("coeff_set")
        signed_done = sem("signed_done")
        sum_done = sem("sum_done")
        wc_hi_done = sem("wc_hi_done")
        wc_lo_done = sem("wc_lo_done")
        block_used = sem("block_used")
        y_full = sem("y_full")
        y_hi_done = sem("y_hi_done")
        y_lo_done = sem("y_lo_done")
        h_full = sem("h_full")
        h_hi_done = sem("h_hi_done")
        h_lo_done = sem("h_lo_done")
        z_full = sem("z_full")
        z_done = sem("z_done")

        x_v = x.rearrange("b (s p) d -> b p s d", p=P)
        mask_v = mask.rearrange("b (k p) o -> b k p o", p=P)
        out_v = out.rearrange("b (s p) (h n) -> b s h p n", p=P, n=BANK)
        w0_v = w0.rearrange("(a p) (q c) -> q p a c", p=P, c=W0C)
        w1_v = w1.rearrange("(h a p) (q c) -> h q p a c", p=P, h=NH, c=BANK)
        la_v = lora_a.rearrange("s (k p) r -> s p k r", p=P)
        stages = [w_stage[:, 0], w_stage[:, 1], z_rows[:].rearrange("p g n -> p (g n)")]
        w_chunks = [stages[j % 3].rearrange("p (a c) -> p a c", c=W0C if j < WCH else BANK) for j in range(2 * WCH)]
        t_bank = (0, 1, 1, 0)

        def need(eng, s, n):
            if not (isinstance(n, int) and n <= 0):
                eng.wait_ge(s, n)

        def weight_bank(j):
            if j < WG:
                return z_ps[j % 2]
            return (z_ps + t_ps)[j % 4] if j < WG + KT else y_ps[j % 4]

        def block_read(eng, b, k):
            if k < 0:
                b, k = b - 1, k + KT
            if isinstance(b, int) and b < 0:
                return
            if k == KT - 1:
                eng.wait_ge(y_full, XG * b + XG)
            else:
                eng.wait_ge(block_used, (KT - 1) * b + k + 1)

        block = ctx.enter_context(nc.Block())

        @block.sync
        def _(sp):
            def load_x(b):
                need(sp, xt_ps, XG * b)
                sp.dma_start(x_rows[:], x_v[bass.ds(b, 1)].rearrange("a p s d -> (a p) s d")).then_inc(x_in, 16)

            def load_mask(b, k):
                need(sp, wc_lo_done, KT * b + k - RING + 1)
                sp.dma_start(masks[:, k % RING, :],
                             mask_v[bass.ds(b, 1), k].rearrange("a p o -> (a p) o")).then_inc(mask_in[k % RING], 16)

            def load_weight(j):
                need(sp, wt_ps, 4 * (j - 2))
                src = w0_v[j] if j < WCH else w1_v[(j - WCH) // 2, (j - WCH) % 2]
                sp.dma_start(w_chunks[j], src).then_inc(w_in[j % 3], 16)

            def load_lora(b):
                slot = sp.value_load(ids[0:1, bass.ds(b, 1)], min_val=0, max_val=SLOTS - 1)
                need(sp, lora_lo_done, 4 * b)
                sp.dma_start(a_raw[:], la_v[bass.ds(slot, 1)].rearrange("a p k r -> (a p) k r")).then_inc(lora_in, 16)
                for j in range(6):
                    sp.dma_start(b_raw[j * R:(j + 1) * R, :],
                                 lora_b[bass.ds(slot, 1)].rearrange("a r o -> (a r) o")).then_inc(lora_in, 16)

            for h in range(2):
                sp.dma_start(x_rows[:, :, h * D // 2:(h + 1) * D // 2],
                             x_v[0][:, :, h * D // 2:(h + 1) * D // 2]).then_inc(x_half_in[h], 16)
            load_weight(0)
            load_mask(0, 0)
            load_weight(1)
            for k in range(1, RING):
                load_mask(0, k)
            load_weight(2)
            load_weight(3)
            load_mask(0, 4)
            load_mask(0, 5)
            load_weight(4)
            load_mask(0, 6)
            load_mask(0, 7)
            load_weight(5)
            load_mask(1, 0)
            sp.wait_ge(ids_in, 16)
            load_lora(0)
            load_x(1)
            load_weight(6)
            load_mask(1, 1)
            load_weight(7)
            for k in range(2, KT):
                load_mask(1, k)
            with sp.Fori(1, NB - 1) as b:
                load_lora(b)
                load_x(b + 1)
                for k in range(KT):
                    load_mask(b + 1, k)
            load_lora(NB - 1)

        @block.gpsimd
        def _(pool):
            pool.memset(ident[:], 0.0).then_inc(ident_zero, 1)
            pool.wait_ge(ident_zero, 1)
            pool.affine_select(out=ident[:], in_=ident[:], compare_op=ALU.not_equal, fill=1.0, base=0,
                               pattern=[[-1, P]], channel_multiplier=1).then_inc(ident_done, 1)
            pool.wait_ge(consts_in, 32)
            pool.tensor_scalar(coeff_pairs[:, :, 0], coeff_all[:], 2.0, None, ALU.mult).then_inc(pairs_done, 1)
            pool.tensor_scalar(coeff_pairs[:, :, 1], coeff_all[:], -1.0, None, ALU.mult).then_inc(pairs_done, 1)
            pool.wait_ge(ident_done, 1)

            def raise_diagonal(j):
                pool.wait_ge(w_in[j % 3], 16 * (j // 3 + 1))
                if j < WCH:
                    per = W0C // P
                    blocks = [w_chunks[j][:, j * per + n, n * P:(n + 1) * P] for n in range(per)]
                else:
                    h, q = divmod(j - WCH, 2)
                    blocks = [w_chunks[j][:, n, n * P:(n + 1) * P] for n in range(BANK // P)] if h == q else []
                for blk in blocks:
                    pool.tensor_tensor(blk, blk, ident[:], ALU.add).then_inc(diag_done, 1)

            for j in range(WCH):
                raise_diagonal(j)
            pool.wait_ge(diag_done, 8)
            pool.wait_ge(b1_in, 32)
            pool.tensor_copy(b_stack[LR:KS, :], b_raw[LR:KS, :]).then_inc(b1_done, 1)
            pool.wait_ge(b1_done, 1)
            pool.tensor_tensor(b_stack[LR:KS, :], b_raw[LR:KS, :], b_stack[LR:KS, :].bitcast(F32),
                               ALU.subtract).then_inc(b1_done, 1)
            pool.wait_ge(b1_done, 2)
            pool.tensor_copy(b_stack[LR:LR + 1, :], b_raw[LR:LR + 1, :]).then_inc(b1_done, 1)
            pool.wait_ge(b1_done, 3)
            for j in range(WCH, 2 * WCH):
                raise_diagonal(j)

            def lora_low(b):
                pool.wait_ge(lora_hi_done, 4 * (b + 1))
                for n in range(3):
                    pool.tensor_tensor(a_parts[:, :, n, R:2 * R], a_raw[:],
                                       a_parts[:, :, n, 0:R].bitcast(F32), ALU.subtract).then_inc(lora_lo_done, 1)
                pool.wait_ge(lora_lo_done, 4 * b + 3)
                pool.tensor_tensor(b_stack[4 * R:LR, :], b_raw[4 * R:LR, :],
                                   b_stack[4 * R:LR, :].bitcast(F32), ALU.subtract).then_inc(lora_lo_done, 1)

            with pool.Fori(0, NB) as b:
                lora_low(b)

        @block.tensor
        def _(pe):
            def weight_group(j):
                c, g = divmod(j, 4)
                if g == 0:
                    pe.wait_ge(w_in[c % 3], 16 * (c // 3 + 1))
                    pe.wait_ge(diag_done, (2, 4, 6, 8, 12, 12, 12, 16)[c])
                bank = weight_bank(j)
                if j < WG + 2:
                    need(pe, (w0_left, w0_right)[j % 2], j // 2)
                elif j < WG + 4:
                    pe.wait_ge(x_lo_done, XG)
                elif WG + KT <= j < WG + KT + 4:
                    pe.wait_ge(y_lo_done, PAIR * (j - WG - KT + 1))
                else:
                    pe.wait_ge(w1_lo_done, j - WG - 3)
                for n in range(4):
                    blk = (w_chunks[c][:, (g % 2) * 4 + n, (g // 2) * P:(g // 2 + 1) * P] if c < WCH
                           else w_chunks[c][:, n, g * P:(g + 1) * P])
                    ins = pe.transpose(bank[:, n * P:(n + 1) * P], blk, ident[:])
                ins.then_inc(wt_ps, 1)

            def x_group(b, g):
                if isinstance(b, int) and b == 0:
                    pe.wait_ge(x_half_in[g // 2], 16)
                elif g == 0:
                    pe.wait_ge(x_in, 16 * b)
                if isinstance(b, int) and b == 1 and g < 2:
                    pe.wait_ge(w1_lo_done, 7 + g)
                if g == 2:
                    pe.wait_ge(x_lo_done, XG * b + 2)
                if g == 3:
                    pe.wait_ge(x_lo_done, XG * b + 1)
                    need(pe, h_lo_done, b)
                bank = t_ps[t_bank[g]]
                for n in range(PAIR):
                    for s in range(ST):
                        ins = pe.transpose(bank[:, n * T + s * P:n * T + (s + 1) * P],
                                           x_rows[:, s, (PAIR * g + n) * P:(PAIR * g + n + 1) * P], ident[:])
                ins.then_inc(xt_ps, 1)

            def layer0_block(b, k):
                if k == 0:
                    pe.wait_ge(x_lo_done, XG * (b + 1))
                    need(pe, y_lo_done, KT * b)
                pe.wait_ge(wc_lo_done, KT * b + k + 1)
                for o in range(KT):
                    acc = y_ps[o // PAIR][:, (o % PAIR) * T:(o % PAIR + 1) * T]
                    for n, (w, xs) in enumerate(((wc_hi, x_hi), (wc_hi, x_lo), (wc_lo, x_hi))):
                        ins = pe.matmul(acc, w[:, k % RING, o * P:(o + 1) * P], xs[:, k, :],
                                        start=(k == 0 and o % PAIR == 0 and n == 0),
                                        stop=(k == KT - 1 and n == 2), skip_group_check=True)
                    if k == KT - 1 and o % PAIR == PAIR - 1:
                        ins.then_inc(y_full, 1)
                if k < KT - 1:
                    ins.then_inc(block_used, 1)

            def layer1_group(b, g, ks=range(KT), first=False):
                s, h = g % ST, g // ST
                if g == 0 and first:
                    pe.wait_ge(w1_lo_done, WG // 2)
                if g == 2 and first:
                    pe.wait_ge(w1_lo_done, WG)
                if ks[0] == 0:
                    need(pe, z_done, OG * b + g - 1)
                for k in ks:
                    if g == 0:
                        pe.wait_ge(y_lo_done, KT * b + k + 1)
                    for n, (ys, w) in enumerate(((y_hi, w1_hi), (y_hi, w1_lo), (y_lo, w1_hi))):
                        pe.matmul(z_ps[g % 2][:], ys[:, k, s * P:(s + 1) * P], w[:, k, h * BANK:(h + 1) * BANK],
                                  start=(k == 0 and n == 0), stop=False)

            def lora_hidden(b, first, last):
                if first:
                    pe.wait_ge(ones_done, 1)
                    pe.wait_ge(b1_done, 3)
                pe.wait_ge(lora_lo_done, 4 * (b + 1))
                if not last:
                    pe.wait_ge(x_lo_done, XG * (b + 1) + 1)
                for k in range(KT):
                    for n, ys in enumerate((y_hi, y_lo)):
                        ins = pe.matmul(t_ps[0][0:LR, 0:T], a_parts[:, k].rearrange("p n r -> p (n r)"), ys[:, k, :],
                                        start=(k == 0 and n == 0), stop=(k == KT - 1 and n == 1))
                ins.then_inc(h_full, 1)

            def close_group(b, g):
                s, h = g % ST, g // ST
                if g == 0:
                    pe.wait_ge(h_lo_done, b + 1)
                    pe.wait_ge(h_hi_done, b + 1)
                pe.matmul(z_ps[g % 2][:], h_stack[0:KS, s * P:(s + 1) * P], b_stack[0:KS, h * BANK:(h + 1) * BANK],
                          start=False, stop=True).then_inc(z_full, 1)

            def batch(b, first=False, last=False):
                for k in range(KT):
                    layer0_block(b, k)
                    if first:
                        for j in (range(2 * k + 6, 2 * k + 8) if k < 5 else range(4 * k - 4, 4 * k) if k < 7 else ()):
                            weight_group(j)
                if not last:
                    x_group(b + 1, 0)
                    x_group(b + 1, 1)
                layer1_group(b, 0, first=first)
                if first:
                    for j in range(24, 28):
                        weight_group(j)
                lora_hidden(b, first, last)
                layer1_group(b, 1, range(KT // 2))
                close_group(b, 0)
                if first:
                    for j in range(28, 32):
                        weight_group(j)
                layer1_group(b, 1, range(KT // 2, KT))
                close_group(b, 1)
                if not last:
                    x_group(b + 1, 2)
                    x_group(b + 1, 3)
                for g in (2, 3):
                    layer1_group(b, g, first=first)
                    close_group(b, g)

            pe.wait_ge(ident_done, 1)
            for g in range(XG):
                x_group(0, g)
            for j in range(4):
                weight_group(j)
            pe.wait_ge(consts_in, 32)
            pe.transpose(y_ps[0][:, 0:KT], b0_rows[:], ident[0:KT, 0:KT]).then_inc(b0_ps, 1)
            weight_group(4)
            weight_group(5)
            pe.wait_ge(b0_done, 1)
            batch(0, first=True)
            with pe.Fori(1, NB - 1) as b:
                batch(b)
            batch(NB - 1, last=True)

        @block.scalar
        def _(act):
            def set_coeff(b):
                need(act, signed_done, KT * b)
                act.activation(coeff_now[:], coeff_pairs[:, bass.ds(b, 1), :].rearrange("p a n -> p (a n)"),
                               ACT.Copy).then_inc(coeff_set, 1)
                act.wait_ge(coeff_set, b + 1)

            def signed_mask(b, k):
                act.wait_ge(mask_in[k % RING], 16 * (2 * b + k // RING + 1))
                act.activation(sums[:, k % RING, :], masks[:, k % RING, :], ACT.Identity,
                               bias=coeff_now[:, 1:2], scale=coeff_now[:, 0:1]).then_inc(signed_done, 1)

            def weights_high(b, k):
                act.wait_ge(sum_done, KT * b + k + 1)
                block_read(act, b, k - RING)
                act.activation(wc_hi[:, k % RING, :], sums[:, k % RING, :], ACT.Copy).then_inc(wc_hi_done, 1)

            def step(b, k, more=True):
                if k < KT - 1:
                    signed_mask(b, k + 1)
                elif more:
                    set_coeff(b + 1)
                    signed_mask(b + 1, 0)
                weights_high(b, k)

            def x_high(b, g):
                act.wait_ge(xt_ps, XG * b + g + 1)
                act.activation(x_hi[:, PAIR * g:PAIR * (g + 1), :], t_ps[t_bank[g]][:].rearrange(
                    "p (n t) -> p n t", n=PAIR), ACT.Copy).then_inc(x_hi_done, 1)

            def w0_left_copy(k):
                act.wait_ge(wt_ps, 2 * k + 1)
                act.activation(w0_t[:, k, 0:BANK], weight_bank(2 * k)[:], ACT.Copy).then_inc(w0_left, 1)

            def w1_high(j):
                act.wait_ge(wt_ps, j + 1)
                h, k = divmod(j - WG, KT)
                act.activation(w1_hi[:, k, h * BANK:(h + 1) * BANK], weight_bank(j)[:],
                               ACT.Copy).then_inc(w1_hi_done, 1)

            def y_high(b, g):
                act.wait_ge(y_full, XG * b + g + 1)
                for o in range(PAIR * g, PAIR * (g + 1)):
                    act.activation(y_hi[:, o, :], y_ps[g][:, (o % PAIR) * T:(o % PAIR + 1) * T], ACT.Identity,
                                   bias=b0_cols[:, o:o + 1]).then_inc(y_hi_done, 1)

            def h_high(b):
                act.wait_ge(h_full, b + 1)
                act.activation(h_stack[0:LR, :], t_ps[0][0:LR, 0:T], ACT.Copy, scale=SCALING).then_inc(h_hi_done, 1)

            def z_copy(b, g):
                act.wait_ge(z_full, OG * b + g + 1)
                need(act, z_out[g], 16 * b)
                act.activation(z_rows[:, g, :], z_ps[g % 2][:], ACT.Copy).then_inc(z_done, 1)

            def store(b, g):
                s, h = g % ST, g // ST
                act.wait_ge(z_done, OG * b + g + 1)
                act.dma_start(out_v[bass.ds(b, 1), s, h].rearrange("a p n -> (a p) n"),
                              z_rows[:, g, :]).then_inc(z_out[g], 16)

            def lora_high(b):
                act.wait_ge(lora_in, 16 * 7 * (b + 1))
                need(act, z_full, OG * b)
                for n in range(3):
                    act.activation(a_parts[:, :, n, 0:R], a_raw[:], ACT.Copy).then_inc(lora_hi_done, 1)
                act.activation(b_stack[0:LR, :], b_raw[0:LR, :], ACT.Copy).then_inc(lora_hi_done, 1)

            def batch(b, first=False, last=False):
                for k in range(0 if first else RING, KT):
                    step(b, k, not last and not first)
                    if first and k < KT - 2:
                        w0_left_copy(k + 2)
                    if first and k >= KT - 2:
                        for j in range(4 * k - 8, 4 * k - 4):
                            w1_high(j)
                    if k == RING + 1 and not first:
                        lora_high(b)
                for g in range(XG):
                    y_high(b, g)
                if not last:
                    x_high(b + 1, 0)
                    x_high(b + 1, 1)
                if first:
                    lora_high(b)
                    set_coeff(b + 1)
                    signed_mask(b + 1, 0)
                if not last:
                    step(b + 1, 0)
                    step(b + 1, 1)
                if first:
                    for j in range(24, 28):
                        w1_high(j)
                h_high(b)
                if first:
                    for j in range(28, 32):
                        w1_high(j)
                if not last:
                    step(b + 1, 2)
                z_copy(b, 0)
                store(b, 0)
                z_copy(b, 1)
                if not last:
                    x_high(b + 1, 2)
                    x_high(b + 1, 3)
                store(b, 1)
                if not last:
                    step(b + 1, 3)
                for g in (2, 3):
                    z_copy(b, g)
                    store(b, g)

            act.dma_start(coeff_all[:], coeff.rearrange("(a n) -> a n", a=1).to_broadcast([P, NB])).then_inc(consts_in, 16)
            act.dma_start(b0_rows[:], b0.rearrange("(k p) -> k p", p=P)).then_inc(consts_in, 16)
            act.dma_start(ids[:], slot_ids.rearrange("(a n) -> a n", a=1)).then_inc(ids_in, 16)
            for j in range(2):
                act.dma_start(b_raw[LR + j:LR + j + 1, :], b1.rearrange("(a n) -> a n", a=1)).then_inc(b1_in, 16)
            x_high(0, 0)
            x_high(0, 1)
            act.wait_ge(pairs_done, 2)
            set_coeff(0)
            x_high(0, 2)
            x_high(0, 3)
            signed_mask(0, 0)
            w0_left_copy(0)
            w0_left_copy(1)
            act.wait_ge(b0_ps, 1)
            act.activation(b0_cols[:], y_ps[0][:, 0:KT], ACT.Copy).then_inc(b0_done, 1)
            act.wait_ge(b0_done, 1)
            batch(0, first=True)
            with act.Fori(1, NB - 1) as b:
                batch(b)
            batch(NB - 1, last=True)
            for g in range(OG):
                act.wait_ge(z_out[g], 16 * NB)

        @block.vector
        def _(dve):
            def weights_sum(b, k):
                dve.wait_ge(signed_done, KT * b + k + 1)
                if isinstance(b, int) and b == 0:
                    dve.wait_ge(w0_left, k + 1)
                    dve.wait_ge(w0_right, k + 1)
                dve.tensor_tensor(sums[:, k % RING, :], sums[:, k % RING, :], w0_t[:, k, :],
                                  ALU.add).then_inc(sum_done, 1)

            def weights_low(b, k):
                dve.wait_ge(wc_hi_done, KT * b + k + 1)
                dve.wait_ge(sum_done, KT * b + k + 1)
                dve.tensor_tensor(wc_lo[:, k % RING, :], sums[:, k % RING, :],
                                  wc_hi[:, k % RING, :].bitcast(F32), ALU.subtract).then_inc(wc_lo_done, 1)

            def step(b, k, more=True):
                if k < KT - 1:
                    weights_sum(b, k + 1)
                elif more:
                    weights_sum(b + 1, 0)
                weights_low(b, k)

            def w0_right_copy(k):
                dve.wait_ge(wt_ps, 2 * k + 2)
                dve.tensor_copy(w0_t[:, k, BANK:D], weight_bank(2 * k + 1)[:]).then_inc(w0_right, 1)

            def x_low(b, g):
                dve.wait_ge(x_hi_done, XG * b + g + 1)
                dve.tensor_tensor(x_lo[:, PAIR * g:PAIR * (g + 1), :],
                                  t_ps[t_bank[g]][:].rearrange("p (n t) -> p n t", n=PAIR),
                                  x_hi[:, PAIR * g:PAIR * (g + 1), :].bitcast(F32),
                                  ALU.subtract).then_inc(x_lo_done, 1)

            def w1_low(j):
                dve.wait_ge(w1_hi_done, j - WG + 1)
                h, k = divmod(j - WG, KT)
                dve.tensor_tensor(w1_lo[:, k, h * BANK:(h + 1) * BANK], weight_bank(j)[:],
                                  w1_hi[:, k, h * BANK:(h + 1) * BANK].bitcast(F32),
                                  ALU.subtract).then_inc(w1_lo_done, 1)

            def y_low(b, g):
                dve.wait_ge(y_hi_done, KT * b + PAIR * (g + 1))
                for o in range(PAIR * g, PAIR * (g + 1)):
                    dve.scalar_tensor_tensor(out=y_lo[:, o, :], in0=y_ps[g][:, (o % PAIR) * T:(o % PAIR + 1) * T],
                                             scalar=b0_cols[:, o:o + 1], in1=y_hi[:, o, :].bitcast(F32),
                                             op0=ALU.add, op1=ALU.subtract).then_inc(y_lo_done, 1)

            def h_low(b):
                dve.wait_ge(h_hi_done, b + 1)
                dve.scalar_tensor_tensor(out=h_stack[2 * R:4 * R, :], in0=t_ps[0][2 * R:4 * R, 0:T], scalar=SCALING,
                                         in1=h_stack[2 * R:4 * R, :].bitcast(F32),
                                         op0=ALU.mult, op1=ALU.subtract).then_inc(h_lo_done, 1)

            def batch(b, first=False, last=False):
                for k in range(0 if first else RING, KT):
                    step(b, k, not last and not first)
                    if first and k < KT - 2:
                        w0_right_copy(k + 2)
                    if first and k >= KT - 2:
                        for j in range(4 * k - 8, 4 * k - 4):
                            w1_low(j)
                for g in range(XG):
                    y_low(b, g)
                if not last:
                    x_low(b + 1, 0)
                    x_low(b + 1, 1)
                    if first:
                        weights_sum(b + 1, 0)
                    step(b + 1, 0)
                    step(b + 1, 1)
                if first:
                    for j in range(24, 28):
                        w1_low(j)
                h_low(b)
                if first:
                    for j in range(28, 32):
                        w1_low(j)
                if not last:
                    step(b + 1, 2)
                    x_low(b + 1, 2)
                    x_low(b + 1, 3)
                    step(b + 1, 3)

            dve.memset(h_stack[LR:P, :].bitcast(F32), 1.0).then_inc(ones_done, 1)
            for g in range(XG):
                x_low(0, g)
            w0_right_copy(0)
            weights_sum(0, 0)
            w0_right_copy(1)
            dve.wait_ge(b0_done, 1)
            batch(0, first=True)
            with dve.Fori(1, NB - 1) as b:
                batch(b)
            batch(NB - 1, last=True)


def kernel(x, condB_coeff, itok_B_0_23, mask_Bx4096x4096_ik1, L0_cond_W, L0_cond_b, L1_cond_W, L1_cond_b,
           L1_cond_lora_As, L1_cond_lora_Bs):
    import numpy as np
    import concourse.bacc as bacc
    from concourse.bass_utils import run_bass_kernel_spmd

    nc = bacc.Bacc("TRN2", target_bir_lowering=False, num_devices=1, dynamic_dma_scratch_size=1024)
    given = {"x": x, "coeff": condB_coeff, "slot_ids": itok_B_0_23, "mask": mask_Bx4096x4096_ik1,
             "w0": L0_cond_W, "b0": L0_cond_b, "w1": L1_cond_W, "b1": L1_cond_b,
             "lora_a": L1_cond_lora_As, "lora_b": L1_cond_lora_Bs}
    arrays, args = {}, []
    for name, a in given.items():
        a = np.ascontiguousarray(a)
        arrays[f"in_{name}"] = a
        args.append(nc.dram_tensor(f"in_{name}", a.shape, mybir.dt.from_np(a.dtype), kind="ExternalInput").ap())
    args.append(nc.dram_tensor("out", arrays["in_x"].shape, F32, kind="ExternalOutput").ap())
    cond_residual_two_layers(nc, *args)
    result = run_bass_kernel_spmd(nc, [arrays], core_ids=[0])
    return result.results[0]["out"]
```

```python
from contextlib import ExitStack

import concourse.bass as bass
from concourse import mybir

ALU = mybir.AluOpType
ACT = mybir.ActivationFunctionType
F32 = mybir.dt.float32
F32R = mybir.dt.float32r
I32 = mybir.dt.int32

P = 128
BANK = 512
RING = 4
SCALING = 2.0


def cond_residual_two_layers(nc, x, coeff, slot_ids, mask, w0, b0, w1, b1, lora_a, lora_b, out):
    NB, T, D = x.shape
    SLOTS, _, R = lora_a.shape
    KT = D // P
    ST = T // P
    NH = D // BANK
    PAIR = BANK // T
    XG = KT // PAIR
    NG = 3
    EDGES = (0, 352, 696, R + D)
    WG = 2 * KT
    W1C = 2 * NH
    LR = 4 * R
    KS = LR + 2
    assert PAIR == 2 and ST == 2 and NH == 2 and XG == 4 and LR == 64

    with ExitStack() as ctx:
        def sb(name, shape, dt):
            return ctx.enter_context(nc.sbuf_tensor(name, shape, dt))

        def sem(name):
            return ctx.enter_context(nc.semaphore(name))

        ident = sb("ident", [P, P], F32)
        coeff_all = sb("coeff_all", [P, NB], F32)
        coeff_pairs = sb("coeff_pairs", [P, NB, 2], F32)
        coeff_now = sb("coeff_now", [P, 2], F32)
        ids = sb("ids", [1, NB], I32)
        b0_rows = sb("b0_rows", [KT, P], F32)
        b0_cols = sb("b0_cols", [P, KT], F32)
        w_stage = sb("w_stage", [P, 2, 2 * D], F32)
        w0_t = sb("w0_t", [P, KT, D], F32)
        w1_hi = sb("w1_hi", [P, KT, R + D], F32R)
        w1_lo = sb("w1_lo", [P, KT, R + D], F32R)
        masks = sb("masks", [P, RING, D], I32)
        sums = masks[:].bitcast(F32)
        wc_hi = sb("wc_hi", [P, RING, D], F32R)
        wc_lo = sb("wc_lo", [P, RING, D], F32R)
        x_rows = sb("x_rows", [P, ST, D], F32)
        x_hi = sb("x_hi", [P, KT, T], F32R)
        x_lo = sb("x_lo", [P, KT, T], F32R)
        y_hi = sb("y_hi", [P, KT, T], F32R)
        y_lo = sb("y_lo", [P, KT, T], F32R)
        a_raw = sb("a_raw", [P, KT, R], F32)
        b_raw = sb("b_raw", [P, D], F32)
        b_stack = sb("b_stack", [P, D], F32R)
        h_rows = sb("h_rows", [P, ST, KS], F32R)
        h_stack = sb("h_stack", [KS, T], F32R)
        z_rows = sb("z_rows", [P, ST, D], F32)

        y_ps = [ctx.enter_context(nc.psum_tensor(f"y_ps{j}", [P, BANK], F32)) for j in range(XG)]
        z_ps = [ctx.enter_context(nc.psum_tensor(f"z_ps{j}", [P, BANK], F32)) for j in range(NG)]
        t_ps = ctx.enter_context(nc.psum_tensor("t_ps", [P, BANK], F32))

        consts_in = sem("consts_in")
        ids_in = sem("ids_in")
        b1_in = sem("b1_in")
        x_part_in = [sem(f"x_part_in{g}") for g in range(XG)]
        x_in = sem("x_in")
        w0_in = [sem(f"w0_in{k}") for k in range(KT)]
        w1_in = [sem(f"w1_in{c}") for c in range(W1C)]
        mask_in = [sem(f"mask_in{j}") for j in range(RING)]
        lora_in = sem("lora_in")
        z_out = [sem(f"z_out{s}") for s in range(ST)]
        ident_zero = sem("ident_zero")
        ident_done = sem("ident_done")
        pairs_done = sem("pairs_done")
        b1_done = sem("b1_done")
        ones_done = sem("ones_done")
        table_used = sem("table_used")
        diag_done = sem("diag_done")
        lora_hi_done = sem("lora_hi_done")
        lora_lo_done = sem("lora_lo_done")
        b0_ps = sem("b0_ps")
        b0_done = sem("b0_done")
        wt_ps = sem("wt_ps")
        w0_left = sem("w0_left")
        w0_right = sem("w0_right")
        w1_hi_done = sem("w1_hi_done")
        w1_lo_done = sem("w1_lo_done")
        xt_ps = sem("xt_ps")
        x_hi_done = sem("x_hi_done")
        x_lo_done = sem("x_lo_done")
        coeff_set = sem("coeff_set")
        signed_done = sem("signed_done")
        sum_done = sem("sum_done")
        wc_hi_done = sem("wc_hi_done")
        wc_lo_done = sem("wc_lo_done")
        block_used = sem("block_used")
        y_full = sem("y_full")
        y_hi_done = sem("y_hi_done")
        y_lo_done = sem("y_lo_done")
        h_full = sem("h_full")
        h_hi_done = sem("h_hi_done")
        h_lo_done = sem("h_lo_done")
        ht_ps = sem("ht_ps")
        h_stacked = sem("h_stacked")
        z_full = sem("z_full")
        z_done = sem("z_done")

        x_v = x.rearrange("b (s p) d -> b p s d", p=P)
        mask_v = mask.rearrange("b (k p) o -> b k p o", p=P)
        out_v = out.rearrange("b (s p) n -> b s p n", p=P)
        w0_v = w0.rearrange("(a p) (q c) -> q p a c", p=P, c=P)
        w1_v = w1.rearrange("(h a p) (q c) -> h q p a c", p=P, h=NH, c=BANK)
        la_v = lora_a.rearrange("s (k p) r -> s p k r", p=P)
        stages = [w_stage[:, 0], w_stage[:, 1], z_rows[:].rearrange("p s n -> p (s n)")]
        w0_blocks = [stages[k // 2 % 3][:, k % 2 * D:(k % 2 + 1) * D].rearrange("p (a c) -> p a c", c=P)
                     for k in range(KT)]
        w1_chunks = [stages[(c + 1) % 3].rearrange("p (a c) -> p a c", c=BANK) for c in range(W1C)]

        def need(eng, s, n):
            if not (isinstance(n, int) and n <= 0):
                eng.wait_ge(s, n)

        def weight_bank(j):
            if j < WG:
                return z_ps[j % 2]
            if j < WG + KT - 1:
                return (z_ps + [t_ps])[j % 4 if j < WG + 4 else (j + 1) % 4]
            return y_ps[(j + 1) % 4]

        def w1_groups(c):
            return range(WG + 4 * c, WG + 4 * (c + 1))

        def last_w1_in(bank, before=2 * WG):
            return max(j for j in range(WG, before) if weight_bank(j) is bank) - WG + 1

        def x_bank(b, g):
            if isinstance(b, int) and b == 0:
                return (t_ps, z_ps[2])[g % 2]
            return (t_ps, z_ps[2], t_ps, y_ps[3])[g]

        def block_read(eng, b, k):
            if k < 0:
                b, k = b - 1, k + KT
            if isinstance(b, int) and b < 0:
                return
            if k == KT - 1:
                eng.wait_ge(y_full, XG * b + XG)
            else:
                eng.wait_ge(block_used, (KT - 1) * b + k + 1)

        block = ctx.enter_context(nc.Block())

        @block.sync
        def _(sp):
            def load_x(b):
                need(sp, xt_ps, XG * b)
                sp.dma_start(x_rows[:], x_v[bass.ds(b, 1)].rearrange("a p s d -> (a p) s d")).then_inc(x_in, 16)

            def load_mask(b, k):
                need(sp, wc_lo_done, KT * b + k - RING + 1)
                sp.dma_start(masks[:, k % RING, :],
                             mask_v[bass.ds(b, 1), k].rearrange("a p o -> (a p) o")).then_inc(mask_in[k % RING], 16)

            def load_w0(k):
                need(sp, wt_ps, 2 * (k // 2 * 2 - 4))
                sp.dma_start(w0_blocks[k], w0_v[k]).then_inc(w0_in[k], 16)

            def load_w1(c):
                sp.wait_ge(wt_ps, 4 * (c + 2))
                sp.dma_start(w1_chunks[c], w1_v[c // 2, c % 2]).then_inc(w1_in[c], 16)

            def load_lora(b):
                slot = sp.value_load(ids[0:1, bass.ds(b, 1)], min_val=0, max_val=SLOTS - 1)
                need(sp, lora_lo_done, 2 * b)
                sp.dma_start(a_raw[:], la_v[bass.ds(slot, 1)].rearrange("a p k r -> (a p) k r")).then_inc(lora_in, 16)
                for j in range(4):
                    sp.dma_start(b_raw[j * R:(j + 1) * R, :],
                                 lora_b[bass.ds(slot, 1)].rearrange("a r o -> (a r) o")).then_inc(lora_in, 16)

            XC = D // XG
            for k in range(KT):
                if k % PAIR == 0:
                    g = k // PAIR
                    sp.dma_start(x_rows[:, :, g * XC:(g + 1) * XC],
                                 x_v[0][:, :, g * XC:(g + 1) * XC]).then_inc(x_part_in[g], 16)
                load_w0(k)
                load_mask(0, k)
            sp.wait_ge(ids_in, 16)
            load_lora(0)
            for c in range(W1C):
                load_w1(c)
            load_mask(1, 0)
            load_x(1)
            for k in range(1, KT):
                load_mask(1, k)
            with sp.Fori(1, NB - 1) as b:
                load_lora(b)
                load_x(b + 1)
                for k in range(KT):
                    load_mask(b + 1, k)
            load_lora(NB - 1)

        @block.gpsimd
        def _(pool):
            pool.memset(ident[:], 0.0).then_inc(ident_zero, 1)
            pool.wait_ge(ident_zero, 1)
            pool.affine_select(out=ident[:], in_=ident[:], compare_op=ALU.not_equal, fill=1.0, base=0,
                               pattern=[[-1, P]], channel_multiplier=1).then_inc(ident_done, 1)
            pool.wait_ge(ident_done, 1)

            for k in range(KT):
                pool.wait_ge(w0_in[k], 16)
                blk = w0_blocks[k][:, k, :]
                pool.tensor_tensor(blk, blk, ident[:], ALU.add).then_inc(diag_done, 1)
                if k == 0:
                    pool.wait_ge(consts_in, 32)
                    pool.tensor_scalar(coeff_pairs[:, :, 0], coeff_all[:], 2.0, None, ALU.mult).then_inc(pairs_done, 1)
                    pool.tensor_scalar(coeff_pairs[:, :, 1], coeff_all[:], -1.0, None, ALU.mult).then_inc(pairs_done, 1)

            def raise_w1(c):
                pool.wait_ge(w1_in[c], 16)
                for n in range(4):
                    blk = w1_chunks[c][:, n, n * P:(n + 1) * P]
                    pool.tensor_tensor(blk, blk, ident[:], ALU.add).then_inc(diag_done, 1)

            def lora_low(b):
                pool.wait_ge(lora_hi_done, 2 * (b + 1))
                pool.tensor_tensor(w1_lo[:, :, 0:R], a_raw[:], w1_hi[:, :, 0:R].bitcast(F32),
                                   ALU.subtract).then_inc(lora_lo_done, 1)
                pool.wait_ge(lora_lo_done, 2 * b + 1)
                pool.tensor_tensor(b_stack[2 * R:LR, :], b_raw[2 * R:LR, :],
                                   b_stack[2 * R:LR, :].bitcast(F32), ALU.subtract).then_inc(lora_lo_done, 1)

            raise_w1(0)
            lora_low(0)
            pool.wait_ge(lora_lo_done, 2)
            raise_w1(3)
            pool.wait_ge(diag_done, KT + 8)
            pool.wait_ge(b1_in, 32)
            pool.tensor_copy(b_stack[LR:KS, :], b_raw[LR:KS, :]).then_inc(b1_done, 1)
            pool.wait_ge(b1_done, 1)
            pool.tensor_tensor(b_stack[LR:KS, :], b_raw[LR:KS, :], b_stack[LR:KS, :].bitcast(F32),
                               ALU.subtract).then_inc(b1_done, 1)
            pool.wait_ge(b1_done, 2)
            pool.tensor_copy(b_stack[LR:LR + 1, :], b_raw[LR:LR + 1, :]).then_inc(b1_done, 1)
            pool.wait_ge(b1_done, 3)
            with pool.Fori(1, NB) as b:
                lora_low(b)

        @block.tensor
        def _(pe):
            def warm_up(n):
                for _ in range(n):
                    pe.transpose(y_ps[3][:, 0:P], ident[:], ident[:])

            def weight_group(j):
                if j < WG:
                    k, h = divmod(j, 2)
                    src = [w0_blocks[k][:, 4 * h + n, :] for n in range(4)]
                    if h == 0:
                        pe.wait_ge(w0_in[k], 16)
                        pe.wait_ge(diag_done, k + 1)
                else:
                    c, g = divmod(j - WG, 4)
                    src = [w1_chunks[c][:, n, g * P:(g + 1) * P] for n in range(4)]
                    if g == 0:
                        pe.wait_ge(w1_in[c], 16)
                        pe.wait_ge(diag_done, KT + (4, 4, 4, 8)[c])
                bank = weight_bank(j)
                if j < WG + 2:
                    need(pe, (w0_left, w0_right)[j % 2], j // 2)
                elif j < WG + 4:
                    pe.wait_ge(x_lo_done, XG)
                elif j < WG + KT - 1:
                    pe.wait_ge(w1_lo_done, j - WG - 2)
                elif j < WG + KT + 3:
                    pe.wait_ge(y_lo_done, PAIR * (j - WG - KT + 2))
                else:
                    pe.wait_ge(w1_lo_done, j - WG - 3)
                if j == WG + KT + 7:
                    pe.wait_ge(h_stacked, 1)
                for n in range(4):
                    ins = pe.transpose(bank[:, n * P:(n + 1) * P], src[n], ident[:])
                ins.then_inc(wt_ps, 1)

            def x_group(b, g, first=False):
                if isinstance(b, int) and b == 0:
                    pe.wait_ge(x_part_in[g], 16)
                elif g == 0:
                    pe.wait_ge(x_in, 16 * b)
                if first:
                    if b == 0:
                        need(pe, x_lo_done, g - 1)
                    else:
                        pe.wait_ge(w1_lo_done, last_w1_in(x_bank(b, g)))
                if g == 1 and not (first and b == 0):
                    need(pe, z_done, NG * ST * (b - 1))
                if g == 2 and not (first and b == 0):
                    pe.wait_ge(x_lo_done, XG * b + 1)
                bank = x_bank(b, g)
                for n in range(PAIR):
                    for s in range(ST):
                        ins = pe.transpose(bank[:, n * T + s * P:n * T + (s + 1) * P],
                                           x_rows[:, s, (PAIR * g + n) * P:(PAIR * g + n + 1) * P], ident[:])
                ins.then_inc(xt_ps, 1)

            def layer0_block(b, k, part="all"):
                if isinstance(b, int) and b == 0 and k % PAIR == 0:
                    pe.wait_ge(x_lo_done, k // PAIR + 1)
                elif k == 0:
                    pe.wait_ge(x_lo_done, XG * (b + 1))
                if k == 0:
                    need(pe, y_lo_done, KT * b)
                products = ((wc_hi, x_hi), (wc_hi, x_lo), (wc_lo, x_hi))
                if part == "high":
                    pe.wait_ge(wc_hi_done, KT * b + k + 1)
                    order = [(o, n) for o in range(KT) for n in range(2)]
                else:
                    pe.wait_ge(wc_lo_done, KT * b + k + 1)
                    order = [(o, n) for o in range(KT) for n in ((2,) if part == "low" else range(3))]
                for o, n in order:
                    w, xs = products[n]
                    ins = pe.matmul(y_ps[o // PAIR][:, (o % PAIR) * T:(o % PAIR + 1) * T],
                                    w[:, k % RING, o * P:(o + 1) * P], xs[:, k, :],
                                    start=(k == 0 and o % PAIR == 0 and n == 0),
                                    stop=(k == KT - 1 and n == 2), skip_group_check=True)
                    if k == KT - 1 and o % PAIR == PAIR - 1 and n == 2:
                        ins.then_inc(y_full, 1)
                if k < KT - 1 and part != "high":
                    ins.then_inc(block_used, 1)

            def layer1_group(b, s, g, ks=range(KT), first=False, last=False):
                if ks[0] == 0:
                    need(pe, z_done, NG * (ST * b + s - 1) + g + 1)
                    if g == 2 and s == 0 and not last:
                        pe.wait_ge(x_lo_done, XG * (b + 1) + 2)
                    if s == 0 and g == 0:
                        pe.wait_ge(lora_lo_done, 2 * (b + 1))
                if first and s == 0:
                    pe.wait_ge(w1_lo_done, (0, KT, KT)[g] + ks[-1] + 1)
                for k in ks:
                    if s == 0 and g == 0:
                        pe.wait_ge(y_lo_done, KT * b + k + 1)
                    for n, (ys, w) in enumerate(((y_hi, w1_hi), (y_hi, w1_lo), (y_lo, w1_hi))):
                        ins = pe.matmul(z_ps[g][:, 0:EDGES[g + 1] - EDGES[g]], ys[:, k, s * P:(s + 1) * P],
                                        w[:, k, EDGES[g]:EDGES[g + 1]],
                                        start=(k == 0 and n == 0), stop=(g == 0 and k == KT - 1 and n == 2),
                                        skip_group_check=True)
                if g == 0 and ks[-1] == KT - 1:
                    ins.then_inc(h_full, 1)

            def turn_h(b, s):
                if isinstance(b, int) and b == 0 and s == 0:
                    pe.wait_ge(ones_done, 1)
                if isinstance(b, int) and b == 0:
                    pe.wait_ge(w1_lo_done, last_w1_in(y_ps[s], WG + 12 if s == 0 else 2 * WG))
                pe.wait_ge(h_hi_done, 2 * (ST * b + s + 1))
                pe.wait_ge(h_lo_done, 2 * (ST * b + s + 1))
                pe.transpose(y_ps[s][0:KS, 0:P], h_rows[:, s, :].bitcast(F32), ident[:]).then_inc(ht_ps, 1)

            def close_group(b, s, g):
                lo = R if g == 0 else 0
                if isinstance(b, int) and b == 0 and s == 0 and g == 0:
                    pe.wait_ge(b1_done, 3)
                if g == 0:
                    pe.wait_ge(h_stacked, ST * b + s + 1)
                pe.matmul(z_ps[g][:, lo:EDGES[g + 1] - EDGES[g]], h_stack[0:KS, s * P:(s + 1) * P],
                          b_stack[0:KS, EDGES[g] + lo - R:EDGES[g + 1] - R],
                          start=False, stop=True, skip_group_check=True).then_inc(z_full, 1)

            def batch(b, first=False, last=False):
                for k in range(KT):
                    if first and k < KT - 1:
                        layer0_block(0, k, "high")
                        for j in range(2 * k + 4, 2 * k + 6) if k + 2 < KT else w1_groups(0):
                            weight_group(j)
                        if k % PAIR == 0 and 0 < k < KT - 2:
                            x_group(0, k // PAIR + 1, True)
                        layer0_block(0, k, "low")
                    else:
                        layer0_block(b, k)
                if first:
                    for j in w1_groups(1):
                        weight_group(j)
                if not last and not first:
                    x_group(b + 1, 0)
                    x_group(b + 1, 1)
                layer1_group(b, 0, 0, range(KT // 2), first, last)
                if first:
                    for j in w1_groups(2):
                        weight_group(j)
                layer1_group(b, 0, 0, range(KT // 2, KT), first, last)
                if first:
                    x_group(1, 0, True)
                    x_group(1, 1, True)
                    turn_h(0, 0)
                    for j in w1_groups(3):
                        weight_group(j)
                for s in range(ST):
                    if s > 0:
                        layer1_group(b, s, 0, last=last)
                    layer1_group(b, s, 1, range(KT // 2), first, last)
                    if not first or s > 0:
                        turn_h(b, s)
                    layer1_group(b, s, 1, range(KT // 2, KT), first, last)
                    if not last:
                        x_group(b + 1, 2 + s, first)
                    close_group(b, s, 0)
                    close_group(b, s, 1)
                    layer1_group(b, s, 2, range(KT), first, last)
                    close_group(b, s, 2)

            pe.wait_ge(ident_done, 1)
            warm_up(10)
            x_group(0, 0, True)
            warm_up(5)
            weight_group(0)
            weight_group(1)
            pe.wait_ge(consts_in, 32)
            pe.transpose(y_ps[0][:, 0:KT], b0_rows[:], ident[0:KT, 0:KT]).then_inc(b0_ps, 1)
            warm_up(10)
            weight_group(2)
            weight_group(3)
            x_group(0, 1, True)
            pe.wait_ge(b0_done, 1)
            batch(0, first=True)
            with pe.Fori(1, NB - 1) as b:
                batch(b)
            batch(NB - 1, last=True)

        @block.scalar
        def _(act):
            def set_coeff(b):
                need(act, signed_done, KT * b)
                act.activation(coeff_now[:], coeff_pairs[:, bass.ds(b, 1), :].rearrange("p a n -> p (a n)"),
                               ACT.Copy).then_inc(coeff_set, 1)
                act.wait_ge(coeff_set, b + 1)

            def signed_mask(b, k):
                act.wait_ge(mask_in[k % RING], 16 * (2 * b + k // RING + 1))
                act.activation(sums[:, k % RING, :], masks[:, k % RING, :], ACT.Identity,
                               bias=coeff_now[:, 1:2], scale=coeff_now[:, 0:1]).then_inc(signed_done, 1)

            def weights_high(b, k):
                act.wait_ge(sum_done, KT * b + k + 1)
                block_read(act, b, k - RING)
                act.activation(wc_hi[:, k % RING, :], sums[:, k % RING, :], ACT.Copy).then_inc(wc_hi_done, 1)

            def step(b, k, more=True):
                if k < KT - 1:
                    signed_mask(b, k + 1)
                elif more:
                    set_coeff(b + 1)
                    signed_mask(b + 1, 0)
                weights_high(b, k)

            def x_high(b, g):
                act.wait_ge(xt_ps, XG * b + g + 1)
                act.activation(x_hi[:, PAIR * g:PAIR * (g + 1), :], x_bank(b, g)[:].rearrange(
                    "p (n t) -> p n t", n=PAIR), ACT.Copy).then_inc(x_hi_done, 1)

            def w0_left_copy(k):
                act.wait_ge(wt_ps, 2 * k + 1)
                act.activation(w0_t[:, k, 0:BANK], weight_bank(2 * k)[:], ACT.Copy).then_inc(w0_left, 1)

            def w1_high(j):
                act.wait_ge(wt_ps, j + 1)
                h, k = divmod(j - WG, KT)
                act.activation(w1_hi[:, k, R + h * BANK:R + (h + 1) * BANK], weight_bank(j)[:],
                               ACT.Copy).then_inc(w1_hi_done, 1)

            def y_high(b, g):
                act.wait_ge(y_full, XG * b + g + 1)
                for o in range(PAIR * g, PAIR * (g + 1)):
                    act.activation(y_hi[:, o, :], y_ps[g][:, (o % PAIR) * T:(o % PAIR + 1) * T], ACT.Identity,
                                   bias=b0_cols[:, o:o + 1]).then_inc(y_hi_done, 1)

            def h_high(b, s):
                act.wait_ge(h_full, ST * b + s + 1)
                for n in (0, 2):
                    act.activation(h_rows[:, s, n * R:(n + 1) * R], z_ps[0][:, 0:R], ACT.Copy,
                                   scale=SCALING).then_inc(h_hi_done, 1)

            def h_copy(b, s):
                act.wait_ge(ht_ps, ST * b + s + 1)
                act.activation(h_stack[:, s * P:(s + 1) * P], y_ps[s][0:KS, 0:P], ACT.Copy).then_inc(h_stacked, 1)

            def z_copy(b, s, g):
                act.wait_ge(z_full, NG * (ST * b + s) + g + 1)
                if g == 0:
                    need(act, z_out[s], 16 * b)
                lo = R if g == 0 else 0
                act.activation(z_rows[:, s, EDGES[g] + lo - R:EDGES[g + 1] - R],
                               z_ps[g][:, lo:EDGES[g + 1] - EDGES[g]], ACT.Copy).then_inc(z_done, 1)

            def store(b, s, g0=0, g1=NG):
                act.wait_ge(z_done, NG * (ST * b + s) + g1)
                lo, hi = max(EDGES[g0] - R, 0), EDGES[g1] - R
                act.dma_start(out_v[bass.ds(b, 1), s].rearrange("a p n -> (a p) n")[:, lo:hi],
                              z_rows[:, s, lo:hi]).then_inc(z_out[s], 16)

            def lora_high(b):
                act.wait_ge(lora_in, 16 * 5 * (b + 1))
                need(act, z_full, NG * ST * b)
                act.activation(w1_hi[:, :, 0:R], a_raw[:], ACT.Copy).then_inc(lora_hi_done, 1)
                act.activation(b_stack[0:LR, :], b_raw[0:LR, :], ACT.Copy).then_inc(lora_hi_done, 1)

            def batch(b, first=False, last=False):
                if first:
                    w0_left_copy(1)
                    weights_high(0, 0)
                    signed_mask(0, 1)
                    x_high(0, 1)
                    w0_left_copy(2)
                    weights_high(0, 1)
                    signed_mask(0, 2)
                    for k in range(2, KT):
                        if k > 2:
                            w0_left_copy(k)
                        if k + 1 < KT:
                            signed_mask(0, k + 1)
                        if k > 2 and k % PAIR == 0:
                            x_high(0, k // PAIR)
                        weights_high(0, k)
                    for j in w1_groups(0):
                        w1_high(j)
                    lora_high(0)
                else:
                    for k in range(RING, KT):
                        step(b, k, not last)
                        if k == RING + 1:
                            lora_high(b)
                for g in range(XG):
                    y_high(b, g)
                if first:
                    for j in (*w1_groups(1), *w1_groups(2)):
                        w1_high(j)
                elif not last:
                    x_high(b + 1, 0)
                    x_high(b + 1, 1)
                    step(b + 1, 0)
                h_high(b, 0)
                if first:
                    x_high(1, 0)
                    h_copy(0, 0)
                    for j in w1_groups(3):
                        w1_high(j)
                    x_high(1, 1)
                    set_coeff(1)
                    signed_mask(1, 0)
                    step(1, 0)
                if not first:
                    h_copy(b, 0)
                if not last:
                    x_high(b + 1, 2)
                    step(b + 1, 1)
                z_copy(b, 0, 0)
                z_copy(b, 0, 1)
                if not last:
                    step(b + 1, 2)
                z_copy(b, 0, 2)
                store(b, 0)
                h_high(b, 1)
                h_copy(b, 1)
                if not last:
                    x_high(b + 1, 3)
                z_copy(b, 1, 0)
                z_copy(b, 1, 1)
                if not last:
                    step(b + 1, 3)
                    z_copy(b, 1, 2)
                    store(b, 1)
                else:
                    store(b, 1, 0, 2)
                    z_copy(b, 1, 2)
                    store(b, 1, 2, 3)

            act.dma_start(coeff_all[:], coeff.rearrange("(a n) -> a n", a=1).to_broadcast([P, NB])).then_inc(consts_in, 16)
            act.dma_start(b0_rows[:], b0.rearrange("(k p) -> k p", p=P)).then_inc(consts_in, 16)
            act.wait_ge(ones_done, 1)
            act.activation(coeff_now[:], h_rows[:, 0, LR:KS].bitcast(F32), ACT.Identity).then_inc(table_used, 1)
            act.wait_ge(table_used, 1)
            act.dma_start(ids[:], slot_ids.rearrange("(a n) -> a n", a=1)).then_inc(ids_in, 16)
            x_high(0, 0)
            act.wait_ge(pairs_done, 2)
            set_coeff(0)
            w0_left_copy(0)
            signed_mask(0, 0)
            for j in range(2):
                act.dma_start(b_raw[LR + j:LR + j + 1, :], b1.rearrange("(a n) -> a n", a=1)).then_inc(b1_in, 16)
            act.wait_ge(b0_ps, 1)
            act.activation(b0_cols[:], y_ps[0][:, 0:KT], ACT.Copy).then_inc(b0_done, 1)
            act.wait_ge(b0_done, 1)
            batch(0, first=True)
            with act.Fori(1, NB - 1) as b:
                batch(b)
            batch(NB - 1, last=True)
            for s in range(ST):
                act.wait_ge(z_out[s], 16 * (NB + s))

        @block.vector
        def _(dve):
            def weights_sum(b, k):
                dve.wait_ge(signed_done, KT * b + k + 1)
                if isinstance(b, int) and b == 0:
                    dve.wait_ge(w0_left, k + 1)
                    dve.wait_ge(w0_right, k + 1)
                dve.tensor_tensor(sums[:, k % RING, :], sums[:, k % RING, :], w0_t[:, k, :],
                                  ALU.add).then_inc(sum_done, 1)

            def weights_low(b, k):
                dve.wait_ge(wc_hi_done, KT * b + k + 1)
                dve.wait_ge(sum_done, KT * b + k + 1)
                dve.tensor_tensor(wc_lo[:, k % RING, :], sums[:, k % RING, :],
                                  wc_hi[:, k % RING, :].bitcast(F32), ALU.subtract).then_inc(wc_lo_done, 1)

            def step(b, k, more=True):
                if k < KT - 1:
                    weights_sum(b, k + 1)
                elif more:
                    weights_sum(b + 1, 0)
                weights_low(b, k)

            def w0_right_copy(k):
                dve.wait_ge(wt_ps, 2 * k + 2)
                dve.tensor_copy(w0_t[:, k, BANK:D], weight_bank(2 * k + 1)[:]).then_inc(w0_right, 1)

            def x_low(b, g):
                dve.wait_ge(x_hi_done, XG * b + g + 1)
                dve.tensor_tensor(x_lo[:, PAIR * g:PAIR * (g + 1), :],
                                  x_bank(b, g)[:].rearrange("p (n t) -> p n t", n=PAIR),
                                  x_hi[:, PAIR * g:PAIR * (g + 1), :].bitcast(F32),
                                  ALU.subtract).then_inc(x_lo_done, 1)

            def w1_low(j):
                dve.wait_ge(w1_hi_done, j - WG + 1)
                h, k = divmod(j - WG, KT)
                dve.tensor_tensor(w1_lo[:, k, R + h * BANK:R + (h + 1) * BANK], weight_bank(j)[:],
                                  w1_hi[:, k, R + h * BANK:R + (h + 1) * BANK].bitcast(F32),
                                  ALU.subtract).then_inc(w1_lo_done, 1)

            def y_low(b, g):
                dve.wait_ge(y_hi_done, KT * b + PAIR * (g + 1))
                for o in range(PAIR * g, PAIR * (g + 1)):
                    dve.scalar_tensor_tensor(out=y_lo[:, o, :], in0=y_ps[g][:, (o % PAIR) * T:(o % PAIR + 1) * T],
                                             scalar=b0_cols[:, o:o + 1], in1=y_hi[:, o, :].bitcast(F32),
                                             op0=ALU.add, op1=ALU.subtract).then_inc(y_lo_done, 1)

            def h_low(b, s):
                dve.wait_ge(h_hi_done, 2 * (ST * b + s + 1))
                for n in (1, 3):
                    dve.scalar_tensor_tensor(out=h_rows[:, s, n * R:(n + 1) * R], in0=z_ps[0][:, 0:R], scalar=SCALING,
                                             in1=h_rows[:, s, 0:R].bitcast(F32),
                                             op0=ALU.mult, op1=ALU.subtract).then_inc(h_lo_done, 1)

            def batch(b, first=False, last=False):
                if first:
                    w0_right_copy(1)
                    weights_low(0, 0)
                    weights_sum(0, 1)
                    x_low(0, 1)
                    w0_right_copy(2)
                    weights_low(0, 1)
                    weights_sum(0, 2)
                    for k in range(2, KT):
                        if k + 1 < KT:
                            w0_right_copy(k + 1)
                            weights_sum(0, k + 1)
                        weights_low(0, k)
                        if k + 1 < KT and (k + 1) % PAIR == 0:
                            x_low(0, (k + 1) // PAIR)
                    for j in w1_groups(0):
                        w1_low(j)
                else:
                    for k in range(RING, KT):
                        step(b, k, not last)
                for g in range(XG):
                    y_low(b, g)
                if first:
                    for j in (*w1_groups(1), *w1_groups(2)):
                        w1_low(j)
                elif not last:
                    x_low(b + 1, 0)
                    x_low(b + 1, 1)
                    step(b + 1, 0)
                h_low(b, 0)
                if first:
                    x_low(1, 0)
                    for j in w1_groups(3):
                        w1_low(j)
                    x_low(1, 1)
                    weights_sum(1, 0)
                    step(1, 0)
                if not last:
                    x_low(b + 1, 2)
                    step(b + 1, 1)
                    step(b + 1, 2)
                h_low(b, 1)
                if not last:
                    x_low(b + 1, 3)
                    step(b + 1, 3)

            dve.memset(h_rows[:, :, LR:KS].bitcast(F32), 1.0).then_inc(ones_done, 1)
            x_low(0, 0)
            w0_right_copy(0)
            weights_sum(0, 0)
            dve.wait_ge(b0_done, 1)
            batch(0, first=True)
            with dve.Fori(1, NB - 1) as b:
                batch(b)
            batch(NB - 1, last=True)


def kernel(x, condB_coeff, itok_B_0_23, mask_Bx4096x4096_ik1, L0_cond_W, L0_cond_b, L1_cond_W, L1_cond_b,
           L1_cond_lora_As, L1_cond_lora_Bs):
    import numpy as np
    import concourse.bacc as bacc
    from concourse.bass_utils import run_bass_kernel_spmd

    nc = bacc.Bacc("TRN2", target_bir_lowering=False, num_devices=1, dynamic_dma_scratch_size=1024)
    given = {"x": x, "coeff": condB_coeff, "slot_ids": itok_B_0_23, "mask": mask_Bx4096x4096_ik1,
             "w0": L0_cond_W, "b0": L0_cond_b, "w1": L1_cond_W, "b1": L1_cond_b,
             "lora_a": L1_cond_lora_As, "lora_b": L1_cond_lora_Bs}
    arrays, args = {}, []
    for name, a in given.items():
        a = np.ascontiguousarray(a)
        arrays[f"in_{name}"] = a
        args.append(nc.dram_tensor(f"in_{name}", a.shape, mybir.dt.from_np(a.dtype), kind="ExternalInput").ap())
    args.append(nc.dram_tensor("out", arrays["in_x"].shape, F32, kind="ExternalOutput").ap())
    cond_residual_two_layers(nc, *args)
    result = run_bass_kernel_spmd(nc, [arrays], core_ids=[0])
    return result.results[0]["out"]
```
